# Optimizing a Trainium2 kernel written in Bass

```python
import numpy as np
import jax
import jax.numpy as jnp

def _softmax(x, axis=-1):
    return jax.nn.softmax(x, axis=axis)

def _gelu(x):
    return jax.nn.gelu(x, approximate=True)

def _silu(x):
    return jax.nn.silu(x)

def _sigmoid(x):
    return jax.nn.sigmoid(x)

def _layernorm(x, axis=-1, eps=1e-05):
    m = jnp.mean(x, axis=axis, keepdims=True)
    v = jnp.var(x, axis=axis, keepdims=True)
    return (x - m) / jnp.sqrt(v + eps)

def _scatter_add(tgt, idx, src, axis=0):
    return tgt.at[idx].add(src)

def _segment_sum(src, seg, n):
    return jax.ops.segment_sum(src, seg, n)
kernel_name = 'mk_audio_tower_d1_tok_audfeat768_r4_e4d5e6'

def setup_inputs(seed: int=0):
    np.random.seed(seed)
    _w = jnp.asarray

    def _rec_inputs():
        import jax
        import jax.numpy as jnp
        _rk = jax.random.key(seed)
        x = -4.65018e-05 + 0.999886 * jax.random.normal(jax.random.fold_in(_rk, 1), (128, 256, 192), jnp.float32)
        return x
    x = _rec_inputs()

    def _L0_tok_setup():
        import jax, jax.numpy as jnp
        import numpy as np
        key = jax.random.key(seed)
        ks = jax.random.split(key, 8)
        B, S, TD, DM = (16, 1024, 192, 192)
        s = 0.02
        return {'text_embeddings': jax.random.normal(ks[0], (B, S, TD), jnp.float32), 'W_w': jax.random.normal(ks[1], (DM, TD), jnp.float32) * s, 'W_b': jax.random.normal(ks[2], (DM,), jnp.float32) * s, 'b': jnp.zeros((DM,), jnp.float32), 'V_w': jax.random.normal(ks[3], (1, DM), jnp.float32) * s, 'V_b': jax.random.normal(ks[4], (1,), jnp.float32) * s, 'P_w': jax.random.normal(ks[5], (DM, TD), jnp.float32) * s, 'P_b': jax.random.normal(ks[6], (DM,), jnp.float32) * s, 'patch_len': 4, 'stride': 2}
    _L0_tok_all = _L0_tok_setup()
    _L0_tok_in = {k: v for k, v in _L0_tok_all.items() if k in ('W_w', 'W_b', 'b', 'V_w', 'V_b', 'P_w', 'P_b')}
    del _L0_tok_all

    def _L0_attn_setup():
        import jax, jax.numpy as jnp
        import numpy as np
        NUM_HEADS = 8

        def _attn(q, k, v, scale):
            a = jax.nn.softmax(jnp.einsum('bhqd,bhkd->bhqk', q, k) * scale, axis=-1)
            return jnp.einsum('bhqk,bhkd->bhqd', a, v)
        key = jax.random.key(seed)
        k1, k2, k3 = jax.random.split(key, 3)
        B, N, C = (8, 256, 192)
        x = jax.random.normal(k1, (B, N, C), dtype=jnp.float32)
        w_qkv = jax.random.normal(k2, (3 * C, C), dtype=jnp.float32) * 0.02
        w_proj = jax.random.normal(k3, (C, C), dtype=jnp.float32) * 0.02
        b_proj = jnp.zeros((C,), dtype=jnp.float32)
        return {'x': x, 'w_qkv': w_qkv, 'w_proj': w_proj, 'b_proj': b_proj}
    _L0_attn_all = _L0_attn_setup()
    _L0_attn_in = {k: v for k, v in _L0_attn_all.items() if k in ('w_qkv', 'w_proj', 'b_proj')}
    del _L0_attn_all

    def _L0_ffn_setup():
        import jax, jax.numpy as jnp
        import numpy as np
        DIM = 192
        HIDDEN = 192
        NUM_EXPERTS = 4
        B, S = (16, 512)
        key = jax.random.key(seed)
        ks = jax.random.split(key, 7)
        sd = 1.0 / np.sqrt(DIM)
        sh = 1.0 / np.sqrt(HIDDEN)
        return {'x': jax.random.normal(ks[0], (B, S, DIM), dtype=jnp.float32), 'router_w': jax.random.uniform(ks[1], (DIM, NUM_EXPERTS), jnp.float32, -sd, sd), 'router_b': jax.random.uniform(ks[2], (NUM_EXPERTS,), jnp.float32, -sd, sd), 'w1': jax.random.uniform(ks[3], (NUM_EXPERTS, DIM, HIDDEN), jnp.float32, -sd, sd), 'b1': jax.random.uniform(ks[4], (NUM_EXPERTS, HIDDEN), jnp.float32, -sd, sd), 'w2': jax.random.uniform(ks[5], (NUM_EXPERTS, HIDDEN, DIM), jnp.float32, -sd, sd), 'b2': jax.random.uniform(ks[6], (NUM_EXPERTS, DIM), jnp.float32, -sd, sd)}
    _L0_ffn_all = _L0_ffn_setup()
    _L0_ffn_in = {k: v for k, v in _L0_ffn_all.items() if k in ('router_w', 'router_b', 'w1', 'b1', 'w2', 'b2')}
    del _L0_ffn_all
    return {'x': x, 'L0_tok_W_w': _L0_tok_in['W_w'], 'L0_tok_W_b': _L0_tok_in['W_b'], 'L0_tok_b': _L0_tok_in['b'], 'L0_tok_V_w': _L0_tok_in['V_w'], 'L0_tok_V_b': _L0_tok_in['V_b'], 'L0_tok_P_w': _L0_tok_in['P_w'], 'L0_tok_P_b': _L0_tok_in['P_b'], 'L0_attn_w_qkv': _L0_attn_in['w_qkv'], 'L0_attn_w_proj': _L0_attn_in['w_proj'], 'L0_attn_b_proj': _L0_attn_in['b_proj'], 'L0_ffn_router_w': _L0_ffn_in['router_w'], 'L0_ffn_router_b': _L0_ffn_in['router_b'], 'L0_ffn_w1': _L0_ffn_in['w1'], 'L0_ffn_b1': _L0_ffn_in['b1'], 'L0_ffn_w2': _L0_ffn_in['w2'], 'L0_ffn_b2': _L0_ffn_in['b2']}

def reference(x, L0_tok_W_w, L0_tok_W_b, L0_tok_b, L0_tok_V_w, L0_tok_V_b, L0_tok_P_w, L0_tok_P_b, L0_attn_w_qkv, L0_attn_w_proj, L0_attn_b_proj, L0_ffn_router_w, L0_ffn_router_b, L0_ffn_w1, L0_ffn_b1, L0_ffn_w2, L0_ffn_b2):
    import jax
    import jax.numpy as jnp

    def _L0_tok_ref(text_embeddings, W_w, W_b, b, V_w, V_b, P_w, P_b, patch_len, stride):
        import jax, jax.numpy as jnp
        import numpy as np
        B, S, TD = text_embeddings.shape
        A = jnp.tanh(jnp.einsum('bst,dt->bsd', text_embeddings, W_w) + W_b + b)
        scores = jnp.einsum('bsd,od->bso', A, V_w)[..., 0] + V_b[0]
        starts = jnp.arange(0, S - patch_len + 1, stride)
        idx = starts[:, None] + jnp.arange(patch_len)
        sw = scores[:, idx]
        w = jax.nn.softmax(sw, axis=-1)
        xw = text_embeddings[:, idx]
        attended = jnp.einsum('bpl,bplt->bpt', w, xw)
        return jnp.einsum('bpt,dt->bpd', attended, P_w) + P_b

    def _L0_attn_ref(x, w_qkv, w_proj, b_proj):
        import jax, jax.numpy as jnp
        import numpy as np
        NUM_HEADS = 8

        def _attn(q, k, v, scale):
            a = jax.nn.softmax(jnp.einsum('bhqd,bhkd->bhqk', q, k) * scale, axis=-1)
            return jnp.einsum('bhqk,bhkd->bhqd', a, v)
        B, N, C = x.shape
        H = NUM_HEADS
        hd = C // H
        g = hd // 3
        scale = hd ** (-0.5)
        qkv = (x @ w_qkv.T).reshape(B, N, 3, H, hd).transpose(2, 0, 3, 1, 4)
        q, k, v = (qkv[0], qkv[1], qkv[2])
        q3, q4, q5 = (q[..., :g], q[..., g:2 * g], q[..., 2 * g:])
        k3, k4, k5 = (k[..., :g], k[..., g:2 * g], k[..., 2 * g:])
        v3, v4, v5 = (v[..., :g], v[..., g:2 * g], v[..., 2 * g:])

        def merge(o):
            return o.transpose(0, 2, 1, 3).reshape(B, N, C // 3)
        x3 = merge(_attn(q4, jnp.concatenate([k3, k4], axis=2), jnp.concatenate([v3, v4], axis=2), scale))
        x4 = merge(_attn(q5, jnp.concatenate([k3, k5], axis=2), jnp.concatenate([v3, v5], axis=2), scale))
        x5 = merge(_attn(q5, jnp.concatenate([k4, k5], axis=2), jnp.concatenate([v4, v5], axis=2), scale))
        out = jnp.concatenate([x3, x4, x5], axis=2)
        return out @ w_proj.T + b_proj

    def _L0_ffn_ref(x, router_w, router_b, w1, b1, w2, b2):
        import jax, jax.numpy as jnp
        import numpy as np
        DIM = 192
        HIDDEN = 192
        NUM_EXPERTS = 4
        B, S = (16, 512)
        logits = jnp.einsum('bsd,de->bse', x, router_w) + router_b
        probs = jax.nn.softmax(logits, axis=-1)
        idx = jnp.argmax(probs, axis=-1)
        dispatch = jax.nn.one_hot(idx, NUM_EXPERTS, dtype=x.dtype)
        h = jnp.einsum('bsd,edh->besh', x, w1) + b1[None, :, None, :]
        h = jax.nn.gelu(h, approximate=False)
        y = jnp.einsum('besh,ehd->besd', h, w2) + b2[None, :, None, :]
        out = jnp.einsum('besd,bse->bsd', y, dispatch)
        out = out + x
        return out
    h = _L0_tok_ref(x, L0_tok_W_w, L0_tok_W_b, L0_tok_b, L0_tok_V_w, L0_tok_V_b, L0_tok_P_w, L0_tok_P_b, 4, 2)
    h = h + _L0_attn_ref(_layernorm(h, axis=-1), L0_attn_w_qkv, L0_attn_w_proj, L0_attn_b_proj)
    h = h + _L0_ffn_ref(_layernorm(h, axis=-1), L0_ffn_router_w, L0_ffn_router_b, L0_ffn_w1, L0_ffn_b1, L0_ffn_w2, L0_ffn_b2)
    return h

_drawn_inputs = setup_inputs


def setup_inputs(seed=0):
    import zlib

    import numpy as np

    out = dict(_drawn_inputs(seed))
    spreads = {'L0_tok_b': (0.0, 2.0), 'L0_attn_b_proj': (0.0, 0.1)}
    factors = {'L0_tok_W_b': 43.384, 'L0_ffn_b1': 4.532}
    for name, (base, spread) in spreads.items():
        noise = np.random.default_rng([zlib.crc32(name.encode()), seed]).standard_normal(out[name].shape)
        drawn = base * np.exp(spread * noise) if base else spread * noise
        out[name] = jnp.asarray(drawn.astype(out[name].dtype))
    for name, factor in factors.items():
        out[name] = (out[name] * factor).astype(out[name].dtype)
    return out
```

```python
import numpy as np
import concourse.bass as bass
from concourse import mybir
from contextlib import ExitStack

F32 = mybir.dt.float32
F16 = mybir.dt.float16
BF16 = mybir.dt.bfloat16
ALU = mybir.AluOpType
ACT = mybir.ActivationFunctionType
AX = mybir.AxisListType

C = 192
CA, CB = 128, 64
NT = 128
NP = 127
S = 256
HEADS, GRP, QUAD = 8, 2, 4
G8 = C // HEADS // 3
SCALE = float(C // HEADS) ** -0.5
EPS = 1e-5
NE = 4
HID = 192
HCH = NE * HID // 128
FAR = 2.0 ** 60
G = 4


def seen(count):
    return max(count, 0) if isinstance(count, int) else count


def within(x, n):
    return not isinstance(x, int) or 0 <= x < n


def matmul_split(nc, out, x, w, start=True, stop=True):
    xa, xl, xb = x
    wa, wl, wb, wbl = w
    nc.tensor.matmul(out, xa, wa, start=start, stop=False)
    nc.tensor.matmul(out, xa, wl, start=False, stop=False)
    nc.tensor.matmul(out, xl, wa, start=False, stop=False)
    nc.tensor.matmul(out, xb, wb, start=False, stop=False)
    return nc.tensor.matmul(out, xb, wbl, start=False, stop=stop)


class Tensors:
    pass


def setup(nc, t, dram):
    with ExitStack() as ctx:
        sb = lambda name, shape, dt: ctx.enter_context(nc.sbuf_tensor(name, shape, dt))
        sem = lambda name: ctx.enter_context(nc.semaphore(name))
        splits = []
        for name, n in (("wqkv", 512), ("wproj", C), ("wrouter", NE), ("w1", NE * HID)):
            splits.append((name, n, sb(name + "_a", [CA, n], F32), sb(name + "_b", [128, n], F32)))
        b2f = sb("b2f", [2 * NE, C], F32)
        loaded, zeroed, built, high = sem("weights_loaded"), sem("zeroed"), sem("matrices_built"), sem("high_made")
        block = ctx.enter_context(nc.Block())
        loads = []
        for name, n, a, b in splits:
            src = dram[name]
            loads += [(a[:, :], src[0:CA, :]), (b[0:CB, :], src[CA:C, :]), (b[CB:128, :], src[CA:C, :])]
        loads += [(b2f[:, :], dram["b2"]),
                  (t.wt_a[:, :], dram["wt"][0:CA, :]), (t.wt_b[:, :], dram["wt"][CA:C + 2, :]),
                  (t.pt_a[:, :], dram["pt"][0:CA, :]), (t.pt_b[:, :], dram["pt"][CA:C + 1, :]),
                  (t.vw[:, :], dram["vw"]), (t.vb[:, :], dram["vb"]), (t.bproj[:, :], dram["bproj"]),
                  (t.brouter[:, :], dram["brouter"]), (t.b1[:, :], dram["b1"]),
                  (t.w2[:, :, :], dram["w2"].rearrange("(c p) d -> p c d", p=128))]

        @block.sync
        def _(sp):
            for dst, src in loads:
                sp.dma_start(dst, src).then_inc(loaded, 16)
            sp.wait_ge(loaded, 16 * len(loads))

        @block.gpsimd
        def _(pool):
            n = 0

            def diagonal(m, base, value=1.0):
                nonlocal n
                nc.gpsimd.memset(m[:, :], 0.0).then_inc(zeroed, 1)
                n += 1
                pool.wait_ge(zeroed, n)
                nc.gpsimd.affine_select(out=m[:, :], in_=m[:, :], compare_op=ALU.not_equal, fill=value, base=base,
                                        pattern=[[-1, 128]], channel_multiplier=1).then_inc(built, 1)

            diagonal(t.ident, 0)
            diagonal(t.ident16, 0)
            diagonal(t.below, -1)
            diagonal(t.above, 1)
            nc.gpsimd.memset(t.far[:, :], FAR).then_inc(zeroed, 1)
            n += 1
            pool.wait_ge(zeroed, n)
            nc.gpsimd.affine_select(out=t.far[:, :], in_=t.far[:, :], compare_op=ALU.is_ge, fill=0.0, base=0,
                                    pattern=[[1, NE * HID]], channel_multiplier=-HID).then_inc(zeroed, 1)
            n += 1
            pool.wait_ge(zeroed, n)
            nc.gpsimd.affine_select(out=t.far[:, :], in_=t.far[:, :], compare_op=ALU.is_ge, fill=0.0, base=HID - 1,
                                    pattern=[[-1, NE * HID]], channel_multiplier=HID).then_inc(built, 1)
            nc.gpsimd.memset(t.half[:, :], -0.5)
            for e in range(NE):
                nc.gpsimd.memset(t.rank[:, :, e:e + 1], float(NE - e))

        @block.vector
        def _(dve):
            dve.wait_ge(loaded, 16 * len(loads))
            n = 0
            for name, _, a, b in splits:
                for src, hi in ((a, t.split[name][0]), (b, t.split[name][2])):
                    nc.vector.tensor_copy(hi[:, :], src[:, :]).then_inc(high, 1)
                    n += 1
            nc.vector.tensor_copy(t.b2_hi[:, :], b2f[:, :]).then_inc(high, 1)
            dve.wait_ge(high, n + 1)
            for name, _, a, b in splits:
                for src, k in ((a, 0), (b, 2)):
                    hi, lo = t.split[name][k], t.split[name][k + 1]
                    nc.vector.tensor_tensor(lo[:, :], src[:, :], hi[:, :], ALU.subtract)
            nc.vector.tensor_tensor(t.b2_lo[:, :], b2f[:, :], t.b2_hi[:, :], ALU.subtract)


def tokenize(nc, t, dram, NB):
    NG = NB // G
    with ExitStack() as ctx:
        sb = lambda name, shape, dt=F32: ctx.enter_context(nc.sbuf_tensor(name, shape, dt))
        ps = lambda name, shape, dt=F32: ctx.enter_context(nc.psum_tensor(name, shape, dt))
        sem = lambda name: ctx.enter_context(nc.semaphore(name))
        xt_a = sb("xt_a", [CA, 2, G, S])
        xt_b = sb("xt_b", [CB + 2, 2, G, S])
        xn = sb("xn", [128, 2, G, 2 * C])
        tanhs = sb("tanhs", [128, 2, 2 * C])
        score = sb("score", [128, 2, G, 4])
        least = sb("least", [128, G])
        shifted = sb("shifted", [128, G, 4])
        expo = sb("expo", [128, G, 4])
        total = sb("total", [128, G])
        inv = sb("inv", [128, G])
        weight = sb("weight", [128, 2, G, 4])
        weight_up = sb("weight_up", [128, 2, G, 2])
        diag = sb("diag", [128, 2, 2, 128])
        band = sb("band", [128, 2, 2, 128])
        att_a = sb("att_a", [CA, 2, 128])
        att_b = sb("att_b", [CB + 1, 2, 128])
        pa = [ps(f"pa{i}", [128, 512]) for i in range(2)]
        pt = [ps(f"pt{i}", [128, 512]) for i in range(2)]
        ph = [ps(f"ph{i}", [128, 512]) for i in range(2)]
        p_down = ps("p_down", [128, 512])
        p_up = ps("p_up", [128, 512])

        xt_in = [sem("xt_in_even"), sem("xt_in_odd")]
        xn_in = [sem("xn_in_even"), sem("xn_in_odd")]
        ones = sem("ones_set")
        pe_a, act_tanh, dve_score = sem("pe_a"), sem("act_tanh"), sem("dve_score")
        pe_down, dve_right, dve_least, dve_shifted = sem("pe_down"), sem("dve_right"), sem("dve_least"), sem("dve_shifted")
        act_exp, dve_total, dve_inv, dve_weight = sem("act_exp"), sem("dve_total"), sem("dve_inv"), sem("dve_weight")
        pe_up, dve_up = sem("pe_up"), sem("dve_up")
        pool_diag, dve_band = sem("pool_diag"), sem("dve_band")
        pe_att, act_att, pe_h, act_h = sem("pe_att"), sem("act_att"), sem("pe_h"), sem("act_h")
        dve_stats = sem("dve_stats")
        block = ctx.enter_context(nc.Block())

        def loop(eng, body):
            for i in range(3):
                body(i, i % 2, i // 2)
            pairs = (NG - 1 - 3) // 2
            with eng.Fori(0, pairs) as j:
                body(j * 2 + 3, 1, j + 1)
                body(j * 2 + 4, 0, j + 2)
            for i in range(3 + 2 * pairs, NG + 3):
                body(i, i % 2, i // 2)

        @block.sync
        def _(sp):
            xt_d, xn_d = dram["xt"], dram["xn"]

            def load_xt(g, par):
                if within(g, NG):
                    sp.wait_ge(pe_a, seen(g * G - 4))
                    for dst, lo, hi in ((xt_a[:, par], 0, CA), (xt_b[0:CB, par], CA, C)):
                        src = xt_d[bass.ds(g, 1), :, lo:hi, :].rearrange("g b c s -> c (g b) s")
                        sp.dma_start(dst, src).then_inc(xt_in[par], 16)

            def load_xn(g, par):
                if within(g, NG):
                    sp.wait_ge(pe_att, seen(g * G - 4))
                    src = xn_d[bass.ds(g, 1), :, :, :].rearrange("g b p n -> p (g b) n")
                    sp.dma_start(xn[:, par], src).then_inc(xn_in[par], 16)

            def body(i, par, half):
                if isinstance(i, int) and i == 0:
                    load_xt(0, 0)
                load_xt(i + 1, 1 - par)
                load_xn(i - 1, 1 - par)
            loop(sp, body)

        @block.tensor
        def _(pe):
            pe.wait_ge(ones, 3)

            def body(i, par, half):
                for k in range(G):
                    n, two = i * G + k, k % 2
                    if within(n, NB):
                        if k == 0:
                            pe.wait_ge(xt_in[par], seen(half * 32 + 32))
                        pe.wait_ge(act_tanh, seen(n - 1))
                        for odd in range(2):
                            o = pa[two][:, odd * C:(odd + 1) * C]
                            nc.tensor.matmul(o, xt_a[:, par, k, odd * 128:(odd + 1) * 128], t.wt_a[:, :], start=True, stop=False)
                            last = nc.tensor.matmul(o, xt_b[:, par, k, odd * 128:(odd + 1) * 128], t.wt_b[:, :], start=False, stop=True)
                        last.then_inc(pe_a, 1)
                    if k == 0 and within(i - 1, NG):
                        pe.wait_ge(dve_score, seen(i * G))
                        nc.tensor.matmul(p_down[:, 0:2 * G], t.below[:, :], score[:, 1 - par, :, 0:2],
                                         start=True, stop=True).then_inc(pe_down, 1)
                    if k == 2 and within(i - 1, NG):
                        pe.wait_ge(dve_weight, seen(i))
                        nc.tensor.matmul(p_up[:, 0:2 * G], t.above[:, :], weight[:, 1 - par, :, 2:4],
                                         start=True, stop=True).then_inc(pe_up, 1)
                    u = n - 2 * G
                    if within(u, NB):
                        if k == 0:
                            pe.wait_ge(xn_in[par], seen(half * 16))
                        pe.wait_ge(dve_band, seen(u + 1))
                        pe.wait_ge(act_att, seen(u - 1))
                        for odd in range(2):
                            nc.tensor.matmul(pt[two][:, 0:128], xn[:, par, k, odd * C:odd * C + CA], band[:, two, odd, :],
                                             start=(odd == 0), stop=(odd == 1), skip_group_check=True)
                        for odd in range(2):
                            last = nc.tensor.matmul(pt[two][0:CB, 128:256], xn[:, par, k, odd * C + CA:(odd + 1) * C], band[:, two, odd, :],
                                                    start=(odd == 0), stop=(odd == 1), skip_group_check=True)
                        last.then_inc(pe_att, 1)
                    u = n - 2 * G - 1
                    if within(u, NB):
                        pe.wait_ge(act_att, seen(u + 1))
                        pe.wait_ge(act_h, seen(u - 1))
                        nc.tensor.matmul(ph[1 - two][:, 0:C], att_a[:, 1 - two, :], t.pt_a[:, :], start=True, stop=False)
                        nc.tensor.matmul(ph[1 - two][:, 0:C], att_b[:, 1 - two, :], t.pt_b[:, :], start=False, stop=True)\
                            .then_inc(pe_h, 1)
            loop(pe, body)

        @block.scalar
        def _(act):
            def body(i, par, half):
                for k in range(G):
                    n, two = i * G + k, k % 2
                    if within(n, NB):
                        act.wait_ge(pe_a, seen(n + 1))
                        act.wait_ge(dve_score, seen(n - 1))
                        nc.scalar.activation(tanhs[:, two, :], pa[two][:, 0:2 * C], ACT.Tanh).then_inc(act_tanh, 1)
                    if k == 1 and within(i - 1, NG):
                        act.wait_ge(dve_shifted, seen(i))
                        nc.scalar.activation(expo[:, :, :], shifted[:, :, :], ACT.Exp).then_inc(act_exp, 1)
                    u = n - 2 * G
                    if within(u, NB):
                        act.wait_ge(pe_att, seen(u + 1))
                        act.wait_ge(pe_h, seen(u - 1))
                        nc.scalar.activation(att_a[:, two, :], pt[two][:, 0:128], ACT.Copy)
                        nc.scalar.activation(att_b[0:CB, two, :], pt[two][0:CB, 128:256], ACT.Copy).then_inc(act_att, 1)
                    u = n - 2 * G - 1
                    if within(u, NB):
                        act.wait_ge(pe_h, seen(u + 1))
                        nc.scalar.activation(t.h[:, bass.ds(u * C, C)], ph[1 - two][:, 0:C], ACT.Copy).then_inc(act_h, 1)
            loop(act, body)

        @block.vector
        def _(dve):
            nc.vector.memset(xt_b[CB:CB + 2, :, :, :], 1.0).then_inc(ones, 1)
            nc.vector.memset(att_b[CB:CB + 1, :, :], 1.0).then_inc(ones, 1)
            nc.vector.memset(expo[:, :, :], 0.0).then_inc(ones, 1)

            def softmax(i, par, step):
                g = i - 1
                if not within(g, NG):
                    return
                if step == 0:
                    dve.wait_ge(pe_down, seen(i))
                    nc.vector.tensor_copy(score[:, par, :, 2:4], p_down[:, 0:2 * G].rearrange("p (b l) -> p b l", l=2))\
                        .then_inc(dve_right, 1)
                    dve.wait_ge(dve_right, seen(i))
                    nc.vector.tensor_reduce(least[:, :], score[:, par, :, :], AX.X, ALU.max, negate=True).then_inc(dve_least, 1)
                    dve.wait_ge(dve_least, seen(i))
                    nc.vector.tensor_tensor(shifted[:, :, :], score[:, par, :, :],
                                            least[:, :].unsqueeze(2).broadcast_to([128, G, 4]), ALU.add).then_inc(dve_shifted, 1)
                elif step == 1:
                    dve.wait_ge(act_exp, seen(i))
                    nc.vector.tensor_reduce(total[:, :], expo[:, :, :], AX.X, ALU.add).then_inc(dve_total, 1)
                    dve.wait_ge(dve_total, seen(i))
                    nc.vector.reciprocal(inv[:, :], total[:, :]).then_inc(dve_inv, 1)
                    dve.wait_ge(dve_inv, seen(i))
                    nc.vector.tensor_tensor(weight[:, par, :, :], expo[:, :, :],
                                            inv[:, :].unsqueeze(2).broadcast_to([128, G, 4]), ALU.mult).then_inc(dve_weight, 1)
                elif step == 2:
                    dve.wait_ge(pe_up, seen(i))
                    nc.vector.tensor_copy(weight_up[:, par, :, :], p_up[:, 0:2 * G].rearrange("p (b l) -> p b l", l=2))\
                        .then_inc(dve_up, 1)

            def body(i, par, half):
                for k in range(G):
                    n, two = i * G + k, k % 2
                    if within(n, NB):
                        dve.wait_ge(act_tanh, seen(n + 1))
                        for odd in range(2):
                            last = nc.vector.tensor_tensor_reduce(out=tanhs[:, two, odd * C:(odd + 1) * C], in0=tanhs[:, two, odd * C:(odd + 1) * C],
                                                                  in1=t.vw[:, :], scale=1.0, scalar=t.vb[:, 0:1], op0=ALU.mult,
                                                                  op1=ALU.add, accum_out=score[:, par, k, odd:odd + 1])
                        last.then_inc(dve_score, 1)
                    softmax(i, 1 - par, k)
                    u = n - 2 * G + 1
                    if within(u, NB):
                        up, kk = (par, k + 1) if k < G - 1 else (1 - par, 0)
                        dve.wait_ge(pool_diag, seen(u + 1))
                        dve.wait_ge(pe_att, seen(u - 1))
                        if k == G - 1:
                            dve.wait_ge(dve_up, seen(i))
                        for odd in range(2):
                            last = nc.vector.scalar_tensor_tensor(out=band[:, 1 - two, odd, :], in0=t.below[:, :],
                                                                  scalar=weight_up[:, up, kk, odd:odd + 1],
                                                                  in1=diag[:, 1 - two, odd, :], op0=ALU.mult, op1=ALU.add)
                        last.then_inc(dve_band, 1)
                    u = n - 2 * G - 1
                    if within(u, NB):
                        dve.wait_ge(act_h, seen(u + 1))
                        nc.vector.bn_stats(t.stats[:, bass.ds(u * 6, 6)], t.h[:, bass.ds(u * C, C)]).then_inc(dve_stats, 1)
            loop(dve, body)

        @block.gpsimd
        def _(pool):
            def body(i, par, half):
                for k in range(G):
                    n, two = i * G + k, k % 2
                    u = n - 2 * G + 1
                    if within(u, NB):
                        up, kk = (par, k + 1) if k < G - 1 else (1 - par, 0)
                        if k == G - 1:
                            pool.wait_ge(dve_weight, seen(i))
                        pool.wait_ge(dve_band, seen(u - 1))
                        nc.gpsimd.tensor_tensor(diag[:, 1 - two, :, :], t.ident[:, :].unsqueeze(1).broadcast_to([128, 2, 128]),
                                                weight[:, up, kk, 0:2].unsqueeze(2).broadcast_to([128, 2, 128]), ALU.mult)\
                            .then_inc(pool_diag, 1)
            loop(pool, body)


def norm_terms(nc, t, NB, name):
    with ExitStack() as ctx:
        sb = lambda n, shape: ctx.enter_context(nc.sbuf_tensor(name + n, shape, F32))
        step, var_made, root_made = (ctx.enter_context(nc.semaphore(name + n)) for n in ("step", "var_made", "root_made"))
        mean, gap, sq, var = (sb(x, [128, NB]) for x in ("mean", "gap", "sq", "var"))
        st = t.stats[:, 0:6 * NB].rearrange("p (b s) -> p b s", s=6)
        block = ctx.enter_context(nc.Block())

        @block.vector
        def _(dve):
            nc.vector.tensor_tensor(mean[:, :], st[:, :, 1], st[:, :, 4], ALU.add)
            nc.vector.tensor_tensor(gap[:, :], st[:, :, 1], st[:, :, 4], ALU.subtract)
            nc.vector.tensor_tensor(var[:, :], st[:, :, 2], st[:, :, 5], ALU.add).then_inc(step, 1)
            dve.wait_ge(step, 1)
            nc.vector.tensor_tensor(sq[:, :], gap[:, :], gap[:, :], ALU.mult)
            nc.vector.tensor_scalar(var[:, :], var[:, :], 1.0 / C, EPS, ALU.mult, ALU.add).then_inc(step, 1)
            dve.wait_ge(step, 2)
            nc.vector.scalar_tensor_tensor(out=var[:, :], in0=sq[:, :], scalar=0.25, in1=var[:, :],
                                           op0=ALU.mult, op1=ALU.add).then_inc(var_made, 1)
            dve.wait_ge(root_made, 1)
            nc.vector.scalar_tensor_tensor(out=t.shift[:, 0:NB], in0=mean[:, :], scalar=-0.5, in1=t.rstd[:, 0:NB],
                                           op0=ALU.mult, op1=ALU.mult)

        @block.gpsimd
        def _(pool):
            pool.wait_ge(var_made, 1)
            nc.gpsimd.tensor_tensor(t.rstd[:, 0:NB], var[:, :], t.half[:, 0:NB], ALU.pow).then_inc(root_made, 1)


def attend(nc, t, NB):
    with ExitStack() as ctx:
        sb = lambda name, shape, dt=F32: ctx.enter_context(nc.sbuf_tensor(name, shape, dt))
        ps = lambda name, shape, dt=F32: ctx.enter_context(nc.psum_tensor(name, shape, dt))
        sem = lambda name: ctx.enter_context(nc.semaphore(name))
        M = 3
        hn = sb("hn", [128, 256])
        x_hi = sb("x_hi", [128, 2, 128], F16)
        x_lo = sb("x_lo", [128, 128], F16)
        qn = sb("qn", [128, M, 3, HEADS, 32], F16)
        kn = sb("kn", [128, M, 3, HEADS, 32], F16)
        vn = sb("vn", [128, M, 3, HEADS, 32])
        kt = sb("kt", [128, M, GRP, 3, 128], F16)
        qt = sb("qt", [128, M, GRP, 2, 128], F16)
        qm = sb("qm", [128, M, GRP, 3, 128], F16)
        top4 = sb("top4", [128, M, HEADS, 4])
        top1 = sb("top1", [128, M, HEADS])
        probs = sb("probs", [128, HEADS, 768])
        ot = sb("ot", [128, 3, 128])
        inv = sb("att_inv", [128, GRP, 3, QUAD])
        att = sb("att", [128, 256])
        y_hi = sb("y_hi", [128, 2, 128], F16)
        y_lo = sb("y_lo", [128, 128], F16)
        p_max = [ps("p_max0", [128, 4, 128]), ps("p_max1", [128, 4, 128])]
        p_max5 = ps("p_max5", [128, 4, 128])
        p_s = [ps("p_s0", [128, 4, 128]), ps("p_s1", [128, 4, 128])]
        p_s5 = ps("p_s5", [128, 4, 128])
        p_o = ps("p_o", [128, 4, 128])
        p_x = ps("p_x", [128, 512])
        p_x16 = p_x[:, :].bitcast(F16)

        consts = sem("consts")
        act_ln, pe_hnt, act_hi, dve_lo = sem("act_ln"), sem("pe_hnt"), sem("act_hi"), sem("dve_lo")
        pe_qkv, act_high, act_v, dve_low, dve_qkn = sem("pe_qkv"), sem("act_high"), sem("act_v"), sem("dve_low"), sem("dve_qkn")
        pe_kt, act_kt, pe_qt, dve_qt = sem("pe_kt"), sem("act_kt"), sem("pe_qt"), sem("dve_qt")
        pe_max = [sem(f"pe_max{h}") for h in range(HEADS)]
        dve_max = [sem(f"dve_max{h}") for h in range(HEADS)]
        dve_max5 = [sem(f"dve_max5{g}") for g in range(GRP)]
        dve_m = [sem(f"dve_m{g}") for g in range(GRP)]
        pe_qm = [sem(f"pe_qm{g}") for g in range(GRP)]
        dve_qm = [sem(f"dve_qm{g}") for g in range(GRP)]
        pe_s = [sem(f"pe_s{h}") for h in range(HEADS)]
        act_e = [sem(f"act_e{h}") for h in range(HEADS)]
        pe_o = [sem(f"pe_o{g}") for g in range(GRP)]
        act_o = [sem(f"act_o{g}") for g in range(GRP)]
        pe_on = [sem(f"pe_on{g}") for g in range(GRP)]
        dve_inv = [sem(f"dve_inv{g}") for g in range(GRP)]
        dve_att = [sem(f"dve_att{g}") for g in range(GRP)]
        pe_att, act_y, dve_y = sem("pe_attt"), sem("act_y"), sem("dve_y")
        pe_proj, pool_bias, dve_h = sem("pe_proj"), sem("pool_bias"), sem("dve_h")
        dve_dup = sem("dve_dup")
        dve_st = sem("dve_st")
        block = ctx.enter_context(nc.Block())

        def loop(eng, body):
            for i in range(-3, 2):
                body(i, i % M)
            triples = (NB - 5) // M
            with eng.Fori(0, triples) as j:
                for r in range(M):
                    body(j * M + (2 + r), (2 + r) % M)
            for i in range(2 + M * triples, NB + 1):
                body(i, i % M)

        @block.tensor
        def _(pe):
            pe.wait_ge(consts, 3)
            wqkv, wproj = t.split["wqkv"], t.split["wproj"]

            last_reader = ((dve_lo, 2), (dve_qm[1], 0), (dve_qkn, 2), (act_kt, 2), (dve_qt, 2), (dve_qm[0], 1), (dve_y, -1), (dve_h, -1))

            def bank_read(i, s):
                while not isinstance(i, int) or i >= -3:
                    i, s = (i, s - 1) if s else (i - 1, HEADS - 1)
                    reader, d = last_reader[s]
                    if within(i + d, NB):
                        return reader, i + d + 1
                return consts, 0

            def shared(i, m, s):
                if s == 0 and within(i + 2, NB):
                    pe.wait_ge(act_ln, seen(i + 3))
                    pe.wait_ge(*bank_read(i, s))
                    nc.tensor.transpose(p_x[:, 0:128], hn[:, 0:128], t.ident[:, :])
                    nc.tensor.transpose(p_x[:, 128:256], hn[:, 128:256], t.ident[:, :]).then_inc(pe_hnt, 1)
                if s == 1 and within(i, NB):
                    pe.wait_ge(*bank_read(i, s))
                    q_with_max(i, m, 1)
                if s == 2 and within(i + 2, NB):
                    pe.wait_ge(dve_lo, seen(i + 3))
                    pe.wait_ge(*bank_read(i, s))
                    matmul_split(nc, p_x[:, :], (x_hi[:, 0, :], x_lo[:, :], x_hi[:, 1, :]),
                                 [w[:, :] for w in wqkv]).then_inc(pe_qkv, 1)
                if s == 3 and within(i + 2, NB):
                    pe.wait_ge(*bank_read(i, s))
                    b = (m + 2) % M
                    for g in range(GRP):
                        for kind in range(3):
                            o = g * 3 + kind
                            last = nc.tensor.transpose(p_x16[:, o * 128:(o + 1) * 128],
                                                       kn[:, b, kind, QUAD * g:QUAD * (g + 1), :].rearrange("p h d -> p (h d)"),
                                                       t.ident16[:, :])
                    last.then_inc(pe_kt, 1)
                if s == 4 and within(i + 2, NB):
                    pe.wait_ge(*bank_read(i, s))
                    b = (m + 2) % M
                    for g in range(GRP):
                        for kind in range(2):
                            o = g * 2 + kind
                            last = nc.tensor.transpose(p_x16[:, o * 128:(o + 1) * 128],
                                                       qn[:, b, kind, QUAD * g:QUAD * (g + 1), :].rearrange("p h d -> p (h d)"),
                                                       t.ident16[:, :])
                    last.then_inc(pe_qt, 1)
                if s == 5 and within(i + 1, NB):
                    pe.wait_ge(*bank_read(i, s))
                    q_with_max(i + 1, (m + 1) % M, 0)
                if s == 6 and within(i - 1, NB):
                    pe.wait_ge(*bank_read(i, s))
                    pe.wait_ge(dve_dup, seen(i))
                    nc.tensor.transpose(p_x[:, 0:128], att[:, 0:128], t.ident[:, :])
                    nc.tensor.transpose(p_x[:, 128:256], att[:, 128:256], t.ident[:, :]).then_inc(pe_att, 1)
                if s == 7 and within(i - 1, NB):
                    pe.wait_ge(*bank_read(i, s))
                    matmul_split(nc, p_x[:, 0:C], (y_hi[:, 0, :], y_lo[:, :], y_hi[:, 1, :]),
                                 [w[:, :] for w in wproj]).then_inc(pe_proj, 1)

            def q_with_max(b, m, g):
                pe.wait_ge(dve_m[g], seen(b + 1))
                for kind in range(3):
                    last = nc.tensor.transpose(p_x16[:, kind * 128:(kind + 1) * 128],
                                               qn[:, m, kind, QUAD * g:QUAD * (g + 1), :].rearrange("p h d -> p (h d)"),
                                               t.ident16[:, :])
                last.then_inc(pe_qm[g], 1)

            def scores(b, m, h):
                g, r = h // QUAD, slice(32 * (h % QUAD), 32 * (h % QUAD) + 32)
                pe.wait_ge(dve_qm[g], seen(b + 1))
                if h >= 2:
                    pe.wait_ge(act_e[h - 2], seen(b + 1))
                else:
                    pe.wait_ge(act_e[h + 6], seen(b))
                k, q = kt[r, m, g], qm[r, m, g]
                nc.tensor.matmul(p_s[h % 2][:, 0:2, :], k[:, 0, :], q[:, 0:2, :], start=True, stop=True, skip_group_check=True)
                nc.tensor.matmul(p_s[h % 2][:, 2:4, :], k[:, 1, :], q[:, 0:3:2, :], start=True, stop=True, skip_group_check=True)
                if h % 2 == 0:
                    pe.wait_ge(act_e[h - 1] if h else act_e[7], seen(b + 1 if h else b))
                else:
                    pe.wait_ge(pe_s[h - 1], seen(b + 1))
                o = 2 * (h % 2)
                nc.tensor.matmul(p_s5[:, o:o + 2, :], k[:, 2, :], q[:, 1:3, :], start=True, stop=True, skip_group_check=True)\
                    .then_inc(pe_s[h], 1)

            def maxima(b, m, h):
                g, r = h // QUAD, slice(32 * (h % QUAD), 32 * (h % QUAD) + 24)
                pe.wait_ge(dve_qt, seen(b + 1))
                pe.wait_ge(act_kt, seen(b + 1))
                if h >= 2:
                    pe.wait_ge(dve_max[h - 2], seen(b + 1))
                else:
                    pe.wait_ge(dve_max[h + 6], seen(b))
                k, q = kt[r, m, g], qt[r, m, g]
                nc.tensor.matmul(p_max[h % 2][:, 0:2, :], q[:, 0, :], k[:, 0:2, :], start=True, stop=True, skip_group_check=True)
                nc.tensor.matmul(p_max[h % 2][:, 2:4, :], q[:, 1, :], k[:, 0:2, :], start=True, stop=True, skip_group_check=True)
                if h % QUAD == 0:
                    pe.wait_ge(dve_max5[1 - g], seen(b + g))
                else:
                    pe.wait_ge(pe_max[h - 1], seen(b + 1))
                nc.tensor.matmul(p_max5[:, h % QUAD, :], q[:, 1, :], k[:, 2, :], start=True, stop=True, skip_group_check=True)\
                    .then_inc(pe_max[h], 1)

            def outputs(b, m, g, half):
                kinds = ((0, 1), (2,))[half]
                if half == 0:
                    pe.wait_ge(act_e[QUAD * g + 3], seen(b + 1))
                    pe.wait_ge(act_v, seen(b + 1))
                    pe.wait_ge(dve_att[1 - g], seen(b + g))
                for kind in kinds:
                    blocks = (slice(0, 2), slice(0, 3, 2), slice(1, 3))[kind]
                    for j in range(QUAD):
                        h = QUAD * g + j
                        last = nc.tensor.matmul(p_o[32 * j:32 * j + 32, blocks, :], vn[0:NP, m, kind, h, :],
                                                probs[0:NP, h, kind * 256:(kind + 1) * 256].rearrange("p (x q) -> p x q", x=2),
                                                start=(kind == 0), stop=(kind == 2), skip_group_check=True)
                if half == 1:
                    last.then_inc(pe_o[g], 1)

            def outputs_back(b, g):
                pe.wait_ge(act_o[g], seen(b + 1))
                for x in range(3):
                    last = nc.tensor.transpose(p_o[:, x, :], ot[:, x, :], t.ident[:, :])
                last.then_inc(pe_on[g], 1)

            def body(i, m):
                for s in range(HEADS):
                    shared(i, m, s)
                    if within(i, NB):
                        scores(i, m, s)
                    if within(i + 1, NB):
                        maxima(i + 1, (m + 1) % M, s)
                    if s < 2 and within(i - 1, NB):
                        outputs(i - 1, (m - 1) % M, 1, s)
                    if s == 2 and within(i - 1, NB):
                        outputs_back(i - 1, 1)
                    if 4 <= s < 6 and within(i, NB):
                        outputs(i, m, 0, s - 4)
                    if s == 6 and within(i, NB):
                        outputs_back(i, 0)
            loop(pe, body)

        @block.scalar
        def _(act):
            def body(i, m):
                b2 = (m + 2) % M
                for s in range(HEADS):
                    if s == 0 and within(i + 2, NB):
                        act.wait_ge(pe_hnt, seen(i + 3))
                        act.wait_ge(pe_qkv, seen(i + 2))
                        nc.scalar.activation(x_hi[:, :, :], p_x[:, 0:256].rearrange("p (a n) -> p a n", a=2), ACT.Copy)\
                            .then_inc(act_hi, 1)
                    if s == 2 and within(i - 1, NB):
                        outputs_out(i - 1, 1)
                    if s == 2 and within(i + 2, NB):
                        act.wait_ge(pe_qkv, seen(i + 3))
                        nc.scalar.activation(qn[:, b2, 0:2, :, 0:G8],
                                             p_x[:, 0:128].rearrange("p (a h d) -> p a h d", a=2, d=G8), ACT.Copy)
                        nc.scalar.activation(kn[:, b2, :, :, 0:G8],
                                             p_x[:, 128:320].rearrange("p (a h d) -> p a h d", a=3, d=G8), ACT.Copy)\
                            .then_inc(act_high, 1)
                        nc.scalar.activation(vn[:, b2, :, :, 0:G8],
                                             p_x[:, 320:512].rearrange("p (a h d) -> p a h d", a=3, d=G8), ACT.Copy)\
                            .then_inc(act_v, 1)
                    if s == 3 and within(i + 2, NB):
                        act.wait_ge(pe_kt, seen(i + 3))
                        nc.scalar.activation(kt[:, b2, :, :, :].rearrange("p g k n -> p (g k n)"), p_x16[:, 0:768], ACT.Copy)\
                            .then_inc(act_kt, 1)
                    if s == 6 and within(i, NB):
                        outputs_out(i, 0)
                    if s == 6 and within(i - 1, NB):
                        act.wait_ge(pe_att, seen(i))
                        nc.scalar.activation(y_hi[:, :, :], p_x[:, 0:256].rearrange("p (a n) -> p a n", a=2), ACT.Copy)\
                            .then_inc(act_y, 1)
                    if within(i, NB):
                        exponentials(i, s)
                    if s == 7 and within(i + 3, NB):
                        b = i + 3
                        act.wait_ge(pe_hnt, seen(i + 3))
                        for o, lo, hi in ((0, 0, C), (C, CA, C)):
                            last = nc.scalar.activation(hn[:, o:o + hi - lo], t.h[:, bass.ds(b * C + lo, hi - lo)], ACT.Identity,
                                                        scale=t.rstd[:, bass.ds(b, 1)], bias=t.shift[:, bass.ds(b, 1)])
                        last.then_inc(act_ln, 1)

            def exponentials(b, h):
                act.wait_ge(pe_s[h], seen(b + 1))
                act.wait_ge(pe_o[h // QUAD], seen(b))
                one = nc.scalar.activation(probs[:, h, 0:512], p_s[h % 2][:, :, :].rearrange("p x n -> p (x n)"), ACT.Exp, scale=SCALE)
                if h % 2 == 0:
                    one.then_inc(act_e[h], 1)
                else:
                    nc.scalar.activation(probs[:, h - 1:h + 1, 512:768],
                                         p_s5[:, :, :].rearrange("p (h x) n -> p h (x n)", h=2), ACT.Exp, scale=SCALE)\
                        .then_inc(act_e[h], 1)

            def outputs_out(b, g):
                act.wait_ge(pe_o[g], seen(b + 1))
                act.wait_ge(pe_on[1 - g], seen(b + g))
                nc.scalar.activation(ot[:, :, :], p_o[:, 0:3, :], ACT.Copy).then_inc(act_o[g], 1)
            loop(act, body)

        @block.vector
        def _(dve):
            nc.vector.memset(qn[:, :, :, :, :].rearrange("p m k h d -> p (m k h d)"), 0.0).then_inc(dve_st, 1)
            nc.vector.memset(kn[:, :, :, :, :].rearrange("p m k h d -> p (m k h d)"), 0.0).then_inc(dve_st, 1)
            nc.vector.memset(vn[:, :, :, :, :].rearrange("p m k h d -> p (m k h d)"), 0.0).then_inc(dve_st, 1)
            dve.wait_ge(dve_st, 3)
            for m in range(M):
                nc.vector.memset(kn[:, m, :, :, 24:25], 1.0)
                last = nc.vector.memset(vn[:, m, :, :, G8:G8 + 1], 1.0)
            last.then_inc(consts, 3)

            def body(i, m):
                b2, b1 = (m + 2) % M, (m + 1) % M
                for s in range(HEADS):
                    if s == 0 and within(i + 2, NB):
                        dve.wait_ge(act_hi, seen(i + 3))
                        nc.vector.tensor_tensor(x_lo[:, :], p_x[:, 0:128], x_hi[:, 0, :], ALU.subtract)
                        nc.vector.tensor_tensor(x_hi[CB:128, 1, :], p_x[CB:128, 128:256], x_hi[CB:128, 1, :], ALU.subtract)\
                            .then_inc(dve_lo, 1)
                    if s == 1 and within(i, NB):
                        max_out(i, m, 1)
                    if s == 2 and within(i + 2, NB):
                        dve.wait_ge(act_v, seen(i + 3))
                        nc.vector.tensor_tensor(qn[:, b2, 0:2, :, 8:16].rearrange("p a h d -> p (a h) d"),
                                                p_x[:, 0:128].rearrange("p (a d) -> p a d", d=G8),
                                                qn[:, b2, 0:2, :, 0:8].rearrange("p a h d -> p (a h) d"), ALU.subtract)
                        nc.vector.tensor_tensor(kn[:, b2, :, :, 16:24].rearrange("p a h d -> p (a h) d"),
                                                p_x[:, 128:320].rearrange("p (a d) -> p a d", d=G8),
                                                kn[:, b2, :, :, 0:8].rearrange("p a h d -> p (a h) d"), ALU.subtract)
                        nc.vector.tensor_copy(kn[:, b2, :, :, 8:16], kn[:, b2, :, :, 0:8])
                        nc.vector.tensor_copy(qn[:, b2, 0:2, :, 16:24], qn[:, b2, 0:2, :, 0:8]).then_inc(dve_low, 1)
                        dve.wait_ge(dve_low, seen(i + 3))
                        nc.vector.tensor_copy(qn[:, b2, 2, :, 0:24], qn[:, b2, 1, :, 0:24]).then_inc(dve_qkn, 1)
                    if s == 3 and within(i - 1, NB):
                        normalize(i - 1, 1)
                    if s == 4 and within(i + 2, NB):
                        dve.wait_ge(pe_qt, seen(i + 3))
                        nc.vector.tensor_copy(qt[:, b2, :, :, :].rearrange("p g k n -> p (g k n)"), p_x16[:, 0:512]).then_inc(dve_qt, 1)
                    if s == 5 and within(i + 1, NB):
                        max_out(i + 1, b1, 0)
                    if s == 6 and within(i - 1, NB):
                        dve.wait_ge(act_y, seen(i))
                        nc.vector.tensor_tensor(y_lo[:, :], p_x[:, 0:128], y_hi[:, 0, :], ALU.subtract)
                        nc.vector.tensor_tensor(y_hi[CB:128, 1, :], p_x[CB:128, 128:256], y_hi[CB:128, 1, :], ALU.subtract)\
                            .then_inc(dve_y, 1)
                    if s == 7 and within(i, NB):
                        normalize(i, 0)
                    if s == 7 and within(i - 1, NB):
                        b = i - 1
                        dve.wait_ge(pe_proj, seen(i))
                        dve.wait_ge(pool_bias, seen(i))
                        nc.vector.tensor_tensor(t.h[:, bass.ds(b * C, C)], p_x[:, 0:C], t.h[:, bass.ds(b * C, C)], ALU.add)\
                            .then_inc(dve_h, 1)
                    if within(i + 1, NB):
                        row_maxima(i + 1, b1, s)
                    if s == 7 and within(i - 1, NB):
                        b = i - 1
                        dve.wait_ge(dve_h, seen(i))
                        nc.vector.bn_stats(t.stats[:, bass.ds(b * 6, 6)], t.h[:, bass.ds(b * C, C)])

            def row_maxima(b, m, h):
                g = h // QUAD
                dve.wait_ge(pe_max[h], seen(b + 1))
                nc.vector.tensor_reduce(top4[:, m, h, :], p_max[h % 2][:, :, 0:NP], AX.X, ALU.max, negate=True).then_inc(dve_max[h], 1)
                if h % QUAD == QUAD - 1:
                    hs = slice(QUAD * g, QUAD * (g + 1))
                    nc.vector.tensor_reduce(top1[:, m, hs], p_max5[:, :, 0:NP], AX.X, ALU.max, negate=True).then_inc(dve_max5[g], 1)
                    dve.wait_ge(dve_max[h], seen(b + 1))
                    dve.wait_ge(dve_max5[g], seen(b + 1))
                    for x, a, c in ((0, top4[:, m, hs, 0], top4[:, m, hs, 1]),
                                    (1, top4[:, m, hs, 2], top1[:, m, hs]),
                                    (2, top4[:, m, hs, 3], top1[:, m, hs])):
                        last = nc.vector.tensor_tensor(qn[:, m, x, hs, 24], a, c, ALU.min)
                    last.then_inc(dve_m[g], 1)

            def max_out(b, m, g):
                dve.wait_ge(pe_qm[g], seen(b + 1))
                nc.vector.tensor_copy(qm[:, m, g, :, :].rearrange("p k n -> p (k n)"), p_x16[:, 0:384]).then_inc(dve_qm[g], 1)

            def normalize(b, g):
                dve.wait_ge(pe_on[g], seen(b + 1))
                on = p_o[:, 0:3, :].rearrange("p x (h d) -> p x h d", d=32)
                nc.vector.reciprocal(inv[:, g, :, :], on[:, :, :, G8]).then_inc(dve_inv[g], 1)
                dve.wait_ge(dve_inv[g], seen(b + 1))
                if g == 0:
                    dve.wait_ge(pe_att, seen(b))
                nc.vector.tensor_tensor(att[:, 0:C].rearrange("p (x h d) -> p x h d", x=3, d=G8)[:, :, QUAD * g:QUAD * (g + 1), :],
                                        on[:, :, :, 0:G8],
                                        inv[:, g, :, :].unsqueeze(3).broadcast_to([128, 3, QUAD, G8]), ALU.mult)\
                    .then_inc(dve_att[g], 1)
                if g == 1:
                    dve.wait_ge(dve_att[1], seen(b + 1))
                    nc.vector.tensor_copy(att[:, C:256], att[:, CA:C]).then_inc(dve_dup, 1)
            loop(dve, body)

        @block.gpsimd
        def _(pool):
            def body(i, m):
                if within(i + 3, NB):
                    b = i + 3
                    pool.wait_ge(act_ln, seen(i + 4))
                    nc.gpsimd.tensor_tensor(t.h[:, bass.ds(b * C, C)], t.h[:, bass.ds(b * C, C)], t.bproj[:, :], ALU.add)\
                        .then_inc(pool_bias, 1)
            loop(pool, body)


def feed_forward(nc, t, dram, NB):
    NG = NB // G
    NW = G * NT
    with ExitStack() as ctx:
        sb = lambda name, shape, dt=F32: ctx.enter_context(nc.sbuf_tensor(name, shape, dt))
        ps = lambda name, shape, dt=F32: ctx.enter_context(nc.psum_tensor(name, shape, dt))
        sem = lambda name: ctx.enter_context(nc.semaphore(name))
        hn = sb("f_hn", [128, 2, 256])
        res = sb("f_res", [128, 2, G, C])
        x_hi = sb("f_hi", [128, 2, 2, G, 128], F16)
        x_lo = sb("f_lo", [128, 2, G, 128], F16)
        logit = sb("logit", [128, G, NE])
        top = sb("top", [128, G])
        ranked = sb("ranked", [128, G, NE])
        best = sb("best", [128, G])
        pick = sb("pick", [128, G, 2, NE], F16)
        pick_t = sb("pick_t", [2 * NE, 2, G, 128], F16)
        gel = sb("gel", [128, HCH, NW])
        out_sb = sb("out_sb", [128, 2, G, C])
        p_t = [ps(f"f_t{i}", [128, 2, 128]) for i in range(2)]
        p_log = ps("f_log", [128, G, NE])
        p_pick = ps("f_pick", [128, 1024], F16)
        p_w = [ps(f"f_w{i}", [128, 512]) for i in range(2)]
        p_y = [ps(f"f_y{i}", [128, 512]) for i in range(2)]

        act_ln, pe_t, act_hi, dve_lo = sem("f_act_ln"), sem("f_pe_t"), sem("f_act_hi"), sem("f_dve_lo")
        pe_log, pool_res = sem("f_pe_log"), sem("f_pool_res")
        steps = [sem(f"f_pick{k}") for k in range(7)]
        dve_pick, pe_pick, dve_pt = sem("f_dve_pick"), sem("f_pe_pick"), sem("f_dve_pt")
        pe_w = [sem(f"f_pe_w{c}") for c in range(HCH)]
        act_g = [sem(f"f_act_g{c}") for c in range(HCH)]
        pe_y, dve_y = sem("f_pe_y"), sem("f_dve_y")
        stored = [sem("stored_even"), sem("stored_odd")]
        block = ctx.enter_context(nc.Block())

        def loop(eng, body):
            for i in range(-1, 3):
                body(i, i % 2, i // 2)
            pairs = (NG - 1 - 3) // 2
            with eng.Fori(0, pairs) as j:
                body(j * 2 + 3, 1, j + 1)
                body(j * 2 + 4, 0, j + 2)
            for i in range(3 + 2 * pairs, NG):
                body(i, i % 2, i // 2)

        @block.tensor
        def _(pe):
            w1, wr = t.split["w1"], t.split["wrouter"]

            def rows_t(i, par, k):
                g, n = i + 1, (i + 1) * G + k
                if not within(g, NG):
                    return
                pe.wait_ge(act_ln, seen(n + 1))
                pe.wait_ge(dve_lo, seen(n - 1))
                nc.tensor.transpose(p_t[k % 2][:, 0, :], hn[:, k % 2, 0:128], t.ident[:, :])
                nc.tensor.transpose(p_t[k % 2][:, 1, :], hn[:, k % 2, 128:256], t.ident[:, :]).then_inc(pe_t, 1)

            def router(i, par):
                g, q = i + 1, 1 - par
                if not within(g, NG):
                    return
                pe.wait_ge(dve_lo, seen(g * G + G))
                pe.wait_ge(steps[0], seen(g))
                for k in range(G):
                    last = matmul_split(nc, p_log[:, k, :], (x_hi[:, q, 0, k, :], x_lo[:, q, k, :], x_hi[:, q, 1, k, :]),
                                        [w[:, :] for w in wr])
                last.then_inc(pe_log, 1)

            def picks_t(i, par):
                g = i + 1
                if not within(g, NG):
                    return
                pe.wait_ge(dve_pick, seen(g + 1))
                pe.wait_ge(dve_pt, seen(g))
                for k in range(G):
                    last = nc.tensor.transpose(p_pick[0:2 * NE, k * 128:(k + 1) * 128],
                                               pick[:, k, :, :].rearrange("p a e -> p (a e)"), t.ident16[:, :])
                last.then_inc(pe_pick, 1)

            def body(i, par, half):
                for c in range(HCH):
                    if within(i, NG):
                        if c == 0:
                            pe.wait_ge(dve_pt, seen(i + 1))
                        if c >= 2:
                            pe.wait_ge(act_g[c - 2], seen(i + 1))
                        else:
                            pe.wait_ge(act_g[c + 4], seen(i))
                        w = [x[:, c * 128:(c + 1) * 128] for x in w1]
                        xa, xl, xb = (v.rearrange("p g n -> p (g n)") for v in (x_hi[:, par, 0], x_lo[:, par], x_hi[:, par, 1]))
                        o = p_w[c % 2][:, :]
                        nc.tensor.matmul(o, w[0], xa, start=True, stop=False)
                        nc.tensor.matmul(o, w[1], xa, start=False, stop=False)
                        nc.tensor.matmul(o, w[0], xl, start=False, stop=False)
                        nc.tensor.matmul(o, w[2], xb, start=False, stop=False)
                        nc.tensor.matmul(o, w[3], xb, start=False, stop=False)
                        nc.tensor.matmul(o, t.far[:, c * 128:(c + 1) * 128], pick_t[:, par].rearrange("p g n -> p (g n)"),
                                         start=False, stop=True).then_inc(pe_w[c], 1)
                    if c < G:
                        rows_t(i, par, c)
                router(i, par)
                for k in range(G):
                    if within(i, NG):
                        n = i * G + k
                        if k == 0:
                            for c in range(HCH):
                                pe.wait_ge(act_g[c], seen(i + 1))
                        pe.wait_ge(dve_y, seen(n - 1))
                        o = p_y[k % 2][:, 0:C]
                        for c in range(HCH):
                            nc.tensor.matmul(o, gel[:, c, k * 128:(k + 1) * 128], t.w2[:, c, :], start=(c == 0), stop=False)
                        nc.tensor.matmul(o, pick_t[:, par, k, :], t.b2_hi[:, :], start=False, stop=False)
                        nc.tensor.matmul(o, pick_t[:, par, k, :], t.b2_lo[:, :], start=False, stop=True).then_inc(pe_y, 1)
                    if k == 2:
                        picks_t(i, par)
            loop(pe, body)

        @block.scalar
        def _(act):
            def norm(i, k):
                n = (i + 1) * G + k
                if within(i + 1, NG):
                    act.wait_ge(pe_t, seen(n - 1))
                    act.wait_ge(pool_res, seen(n - 1))
                    for o, lo, hi in ((0, 0, C), (C, CA, C)):
                        last = nc.scalar.activation(hn[:, k % 2, o:o + hi - lo], t.h[:, bass.ds(n * C + lo, hi - lo)], ACT.Identity,
                                                    scale=t.rstd[:, bass.ds(n, 1)], bias=t.shift[:, bass.ds(n, 1)])
                    last.then_inc(act_ln, 1)

            def high(i, par, k):
                n = (i + 1) * G + k
                if within(i + 1, NG):
                    act.wait_ge(pe_t, seen(n + 1))
                    if k == 0:
                        act.wait_ge(pe_w[HCH - 1], seen(i))
                    nc.scalar.activation(x_hi[:, 1 - par, :, k, :], p_t[k % 2][:, :, :], ACT.Copy).then_inc(act_hi, 1)

            def body(i, par, half):
                for c in range(HCH):
                    if c < G:
                        norm(i, c)
                    if within(i, NG):
                        act.wait_ge(pe_w[c], seen(i + 1))
                        act.wait_ge(pe_y, seen(i * G))
                        nc.scalar.activation(gel[:, c, :], p_w[c % 2][:, :], ACT.Gelu, bias=t.b1[:, c:c + 1]).then_inc(act_g[c], 1)
                    if c < G:
                        high(i, par, c)
            loop(act, body)

        @block.vector
        def _(dve):
            def low(i, par, k):
                n, q = (i + 1) * G + k, 1 - par
                if within(i + 1, NG):
                    dve.wait_ge(act_hi, seen(n + 1))
                    nc.vector.tensor_tensor(x_lo[:, q, k, :], p_t[k % 2][:, 0, :], x_hi[:, q, 0, k, :], ALU.subtract)
                    nc.vector.tensor_tensor(x_hi[CB:128, q, 1, k, :], p_t[k % 2][CB:128, 1, :], x_hi[CB:128, q, 1, k, :],
                                            ALU.subtract).then_inc(dve_lo, 1)

            def choose(i):
                g1 = i + 2
                if not within(i + 1, NG):
                    return
                dve.wait_ge(pe_log, seen(g1))
                nc.vector.tensor_tensor(logit[:, :, :], p_log[:, :, :], t.brouter[:, :, :], ALU.add).then_inc(steps[0], 1)
                dve.wait_ge(steps[0], seen(g1))
                nc.vector.tensor_reduce(top[:, :], logit[:, :, :], AX.X, ALU.max).then_inc(steps[1], 1)
                dve.wait_ge(steps[1], seen(g1))
                nc.vector.tensor_tensor(ranked[:, :, :], logit[:, :, :], top[:, :].unsqueeze(2).broadcast_to([128, G, NE]),
                                        ALU.is_equal).then_inc(steps[2], 1)
                dve.wait_ge(steps[2], seen(g1))
                nc.vector.tensor_tensor(ranked[:, :, :], ranked[:, :, :], t.rank[:, :, :], ALU.mult).then_inc(steps[3], 1)
                dve.wait_ge(steps[3], seen(g1))
                nc.vector.tensor_reduce(best[:, :], ranked[:, :, :], AX.X, ALU.max).then_inc(steps[4], 1)
                dve.wait_ge(steps[4], seen(g1))
                dve.wait_ge(pe_pick, seen(i + 1))
                nc.vector.tensor_tensor(pick[:, :, 1, :], ranked[:, :, :], best[:, :].unsqueeze(2).broadcast_to([128, G, NE]),
                                        ALU.is_equal).then_inc(steps[5], 1)
                dve.wait_ge(steps[5], seen(g1))
                nc.vector.tensor_scalar(pick[:, :, 0, :], pick[:, :, 1, :], -1.0, None, ALU.add).then_inc(dve_pick, 1)

            def body(i, par, half):
                for k in range(G):
                    low(i, par, k)
                choose(i)
                for k in range(G):
                    if within(i, NG):
                        n = i * G + k
                        dve.wait_ge(pe_y, seen(n + 1))
                        dve.wait_ge(pool_res, seen(n + 1))
                        if k == 0:
                            dve.wait_ge(stored[par], seen(half * 16))
                        nc.vector.tensor_tensor(out_sb[:, par, k, :], p_y[k % 2][:, 0:C], res[:, par, k, :], ALU.add)\
                            .then_inc(dve_y, 1)
                    if k == 2 and within(i + 1, NG):
                        dve.wait_ge(pe_pick, seen(i + 2))
                        dve.wait_ge(pe_y, seen(i * G))
                        nc.vector.tensor_copy(pick_t[:, 1 - par].rearrange("p g n -> p (g n)"), p_pick[0:2 * NE, 0:512])\
                            .then_inc(dve_pt, 1)
            loop(dve, body)

        @block.gpsimd
        def _(pool):
            def body(i, par, half):
                for k in range(G):
                    n = (i + 1) * G + k
                    if within(i + 1, NG):
                        pool.wait_ge(act_ln, seen(n + 1))
                        if k == 0:
                            pool.wait_ge(dve_y, seen(i * G))
                        nc.gpsimd.tensor_tensor(res[:, 1 - par, k, :], t.h[:, bass.ds(n * C, C)], hn[:, k % 2, 0:C], ALU.add)\
                            .then_inc(pool_res, 1)
            loop(pool, body)

        @block.sync
        def _(sp):
            def body(i, par, half):
                if within(i, NG):
                    sp.wait_ge(dve_y, seen(i * G + G))
                    dst = dram["out"][bass.ds(i, 1), :, :, :].rearrange("g b p d -> p (g b) d")
                    sp.dma_start(dst, out_sb[0:NP, par, :, :]).then_inc(stored[par], 16)
            loop(sp, body)
            for par in range(2):
                sp.wait_ge(stored[par], 16 * ((NG + 1 - par) // 2))


def audio_tower(nc, dram, NB):
    t = Tensors()
    with ExitStack() as ctx:
        sb = lambda name, shape, dt=F32: ctx.enter_context(nc.sbuf_tensor(name, shape, dt))
        t.h = sb("h", [128, NB * C])
        t.stats = sb("stats", [128, NB * 6])
        t.rstd = sb("rstd", [128, NB])
        t.shift = sb("shift", [128, NB])
        t.half = sb("half", [128, NB])
        t.ident, t.below, t.above = (sb(n, [128, 128]) for n in ("ident", "below", "above"))
        t.ident16 = sb("ident16", [128, 128], F16)
        t.far = sb("far", [2 * NE, NE * HID], BF16)
        t.rank = sb("rank", [128, G, NE])
        t.wt_a, t.wt_b = sb("wt_a", [CA, C]), sb("wt_b", [CB + 2, C])
        t.pt_a, t.pt_b = sb("pt_a", [CA, C]), sb("pt_b", [CB + 1, C])
        t.vw, t.vb, t.bproj = sb("vw", [128, C]), sb("vb", [128, 1]), sb("bproj", [128, C])
        t.brouter = sb("brouter", [128, G, NE])
        t.b1 = sb("b1", [128, HCH])
        t.w2 = sb("w2", [128, HCH, C])
        t.b2_hi, t.b2_lo = (sb(n, [2 * NE, C], F16) for n in ("b2_hi", "b2_lo"))
        t.split = {}
        for name, n in (("wqkv", 512), ("wproj", C), ("wrouter", NE), ("w1", NE * HID)):
            t.split[name] = [sb(f"{name}_{p}", [128, n], F16) for p in ("ahi", "alo", "bhi", "blo")]
        setup(nc, t, dram)
        tokenize(nc, t, dram, NB)
        norm_terms(nc, t, NB, "first_")
        attend(nc, t, NB)
        norm_terms(nc, t, NB, "second_")
        feed_forward(nc, t, dram, NB)


def kernel(x, L0_tok_W_w, L0_tok_W_b, L0_tok_b, L0_tok_V_w, L0_tok_V_b, L0_tok_P_w, L0_tok_P_b,
           L0_attn_w_qkv, L0_attn_w_proj, L0_attn_b_proj, L0_ffn_router_w, L0_ffn_router_b,
           L0_ffn_w1, L0_ffn_b1, L0_ffn_w2, L0_ffn_b2):
    import concourse.bacc as bacc
    from concourse.bass_utils import run_bass_kernel_spmd

    x = np.asarray(x)
    NB = x.shape[0]
    arr = {}
    arr["xn"] = x.reshape(NB // G, G, 128, 2 * C)
    arr["xt"] = x.reshape(NB // G, G, 128, 2, C).transpose(0, 1, 4, 3, 2).reshape(NB // G, G, C, S)
    arr["wt"] = np.concatenate([np.asarray(L0_tok_W_w).T, np.asarray(L0_tok_W_b)[None], np.asarray(L0_tok_b)[None]])
    arr["pt"] = np.concatenate([np.asarray(L0_tok_P_w).T, np.asarray(L0_tok_P_b)[None]])
    arr["vw"] = np.broadcast_to(np.asarray(L0_tok_V_w).reshape(1, C), (128, C))
    arr["vb"] = np.broadcast_to(np.asarray(L0_tok_V_b).reshape(1, 1), (128, 1))
    w = np.asarray(L0_attn_w_qkv).reshape(3, HEADS, 3, G8, C).transpose(4, 0, 2, 1, 3).reshape(C, 3 * C)
    arr["wqkv"] = w[:, C // 3:]
    arr["wproj"] = np.asarray(L0_attn_w_proj).T
    arr["bproj"] = np.broadcast_to(np.asarray(L0_attn_b_proj).reshape(1, C), (128, C))
    arr["wrouter"] = np.asarray(L0_ffn_router_w)
    arr["brouter"] = np.broadcast_to(np.asarray(L0_ffn_router_b).reshape(1, 1, NE), (128, G, NE))
    arr["w1"] = np.asarray(L0_ffn_w1).transpose(1, 0, 2).reshape(C, NE * HID)
    arr["b1"] = np.asarray(L0_ffn_b1).reshape(HCH, 128).T
    arr["w2"] = np.asarray(L0_ffn_w2).reshape(NE * HID, C)
    b2 = np.asarray(L0_ffn_b2)
    arr["b2"] = np.concatenate([np.zeros_like(b2), b2])
    arr = {n: np.ascontiguousarray(a) for n, a in arr.items()}

    nc = bacc.Bacc("TRN2", target_bir_lowering=False, num_devices=1)
    dram = {n: nc.dram_tensor("in_" + n, a.shape, mybir.dt.from_np(a.dtype), kind="ExternalInput").ap() for n, a in arr.items()}
    dram["out"] = nc.dram_tensor("out", (NB // G, G, NP, C), F32, kind="ExternalOutput").ap()
    audio_tower(nc, dram, NB)
    r = run_bass_kernel_spmd(nc, [{"in_" + n: a for n, a in arr.items()}], core_ids=[0])
    return r.results[0]["out"].reshape(NB, NP, C)
```
